# Optimizing a Trainium2 kernel written in Bass

```python
import numpy as np
import jax
import jax.numpy as jnp

def _softmax(x, axis=-1):
    return jax.nn.softmax(x, axis=axis)

def _gelu(x):
    return jax.nn.gelu(x, approximate=True)

def _silu(x):
    return jax.nn.silu(x)

def _sigmoid(x):
    return jax.nn.sigmoid(x)

def _layernorm(x, axis=-1, eps=1e-05):
    m = jnp.mean(x, axis=axis, keepdims=True)
    v = jnp.var(x, axis=axis, keepdims=True)
    return (x - m) / jnp.sqrt(v + eps)

def _scatter_add(tgt, idx, src, axis=0):
    return tgt.at[idx].add(src)

def _segment_sum(src, seg, n):
    return jax.ops.segment_sum(src, seg, n)
kernel_name = 'mk_flamingo_gated_d2_seqx_r4_eed64b'

def setup_inputs(seed: int=0):
    np.random.seed(seed)
    _w = jnp.asarray

    def _rec_inputs():
        import jax
        import jax.numpy as jnp
        _rk = jax.random.key(seed)
        x = -0.0002928 + 1 * jax.random.normal(jax.random.fold_in(_rk, 1), (4, 512, 256), jnp.float32)
        _lenS = 512 - jax.random.randint(jax.random.fold_in(_rk, 7), (4,), 0, max(1, 512 // 4) + 1, jnp.int32)
        _lenS2 = 512 - jax.random.randint(jax.random.fold_in(_rk, 8), (4,), 0, max(1, 512 // 4) + 1, jnp.int32)
        _ctx_1024P = jax.random.normal(jax.random.fold_in(_rk, 11), (4, 16, 256), jnp.float32)
        _ctx_1024c = jax.random.dirichlet(jax.random.fold_in(_rk, 511), 0.3 * jnp.ones((16,), jnp.float32), (4, 512))
        _ctx_1024t = jnp.einsum('bsk,bkd->bsd', _ctx_1024c, _ctx_1024P)
        _ctx_1024t = _ctx_1024t * jax.lax.rsqrt(jnp.mean(jnp.square(_ctx_1024t)) + 1e-12) * 0.953939
        ctx_1024 = -1.39393e-06 + 0.999914 * (_ctx_1024t + 0.3 * jax.random.normal(jax.random.fold_in(_rk, 611), (4, 512, 256), jnp.float32))
        _g = jax.random.normal(jax.random.fold_in(_rk, 9001), (2, 2), jnp.float32)
        _g = jnp.sign(_g) * jnp.maximum(jnp.abs(_g), 1.0) + (_g == 0) * 1.0
        g_xattn = _g[0]
        g_ffn = _g[1]
        return (x, ctx_1024, g_xattn, g_ffn)
    x, ctx_1024, g_xattn, g_ffn = _rec_inputs()

    def _L0_xattn_setup():
        import jax, jax.numpy as jnp
        import numpy as np
        NUM_HEADS = 16
        DIM_MODEL = 256
        DIM_HEAD = DIM_MODEL // NUM_HEADS

        def _split_heads(x, B):
            return x.reshape(B, -1, NUM_HEADS, DIM_HEAD).transpose(0, 2, 1, 3)
        key = jax.random.key(seed)
        ks = jax.random.split(key, 13)
        B, S, D = (2, 512, DIM_MODEL)
        scale = 1.0 / np.sqrt(D)
        inp = {'query': jax.random.normal(ks[0], (B, S, D), jnp.float32), 'key': jax.random.normal(ks[1], (B, S, D), jnp.float32), 'value': jax.random.normal(ks[2], (B, S, D), jnp.float32), 'Wq': jax.random.normal(ks[3], (D, D), jnp.float32) * scale, 'bq': jax.random.normal(ks[4], (D,), jnp.float32) * scale, 'Wk': jax.random.normal(ks[5], (D, D), jnp.float32) * scale, 'bk': jax.random.normal(ks[6], (D,), jnp.float32) * scale, 'Wv': jax.random.normal(ks[7], (D, D), jnp.float32) * scale, 'bv': jax.random.normal(ks[8], (D,), jnp.float32) * scale, 'Wo': jax.random.normal(ks[9], (D, D), jnp.float32) * scale, 'bo': jax.random.normal(ks[10], (D,), jnp.float32) * scale}
        return inp
    _L0_xattn_all = _L0_xattn_setup()
    _L0_xattn_in = {k: v for k, v in _L0_xattn_all.items() if k in ('Wq', 'bq', 'Wk', 'bk', 'Wv', 'bv', 'Wo', 'bo')}
    del _L0_xattn_all

    def _L0_ffn_setup():
        import jax, jax.numpy as jnp
        import numpy as np
        TOP_K = 2
        EPS = 1e-10
        key = jax.random.key(seed)
        k1, k2, k3, k4 = jax.random.split(key, 4)
        B, S, H, E = (4, 512, 256, 8)
        tokens = jax.random.normal(k1, (B, S, H), dtype=jnp.float32)
        router_w = jax.random.normal(k2, (E, H), dtype=jnp.float32) * (1.0 / np.sqrt(H))
        router_b = jax.random.normal(k3, (E,), dtype=jnp.float32) * 0.01
        expert_weights = jax.random.normal(k4, (E, H, H), dtype=jnp.float32) * (1.0 / np.sqrt(H))
        return {'tokens': tokens, 'router_w': router_w, 'router_b': router_b, 'expert_weights': expert_weights}
    _L0_ffn_all = _L0_ffn_setup()
    _L0_ffn_in = {k: v for k, v in _L0_ffn_all.items() if k in ('router_w', 'router_b', 'expert_weights')}
    del _L0_ffn_all

    def _L1_xattn_setup():
        import jax, jax.numpy as jnp
        import numpy as np
        D_MODEL = 256
        H = 16
        D_K = D_MODEL // H
        key = jax.random.key(seed)
        ks = jax.random.split(key, 11)
        B, S = (2, 512)
        scale = 1.0 / np.sqrt(D_MODEL)
        inp = {'query': jax.random.normal(ks[0], (B, S, D_MODEL), jnp.float32), 'key': jax.random.normal(ks[1], (B, S, D_MODEL), jnp.float32), 'value': jax.random.normal(ks[2], (B, S, D_MODEL), jnp.float32), 'Wq': jax.random.normal(ks[3], (D_MODEL, D_MODEL), jnp.float32) * scale, 'bq': jnp.zeros((D_MODEL,), jnp.float32), 'Wk': jax.random.normal(ks[4], (D_MODEL, D_MODEL), jnp.float32) * scale, 'bk': jnp.zeros((D_MODEL,), jnp.float32), 'Wv': jax.random.normal(ks[5], (D_MODEL, D_MODEL), jnp.float32) * scale, 'bv': jnp.zeros((D_MODEL,), jnp.float32), 'Wo': jax.random.normal(ks[6], (D_MODEL, D_MODEL), jnp.float32) * scale, 'bo': jnp.zeros((D_MODEL,), jnp.float32)}
        return inp
    _L1_xattn_all = _L1_xattn_setup()
    _L1_xattn_in = {k: v for k, v in _L1_xattn_all.items() if k in ('Wq', 'bq', 'Wk', 'bk', 'Wv', 'bv', 'Wo', 'bo')}
    del _L1_xattn_all

    def _L1_ffn_setup():
        import jax, jax.numpy as jnp
        import numpy as np
        EMBED_DIM = 256
        HIDDEN = 4 * EMBED_DIM
        BATCH, SEQ = (4, 1024)
        EPS = 1e-05

        def _quant_weight(w):
            s = jnp.clip(jnp.mean(jnp.abs(w)), EPS, None)
            wq = jnp.clip(jnp.round(w / s), -1.0, 1.0) * s
            return w + jax.lax.stop_gradient(wq - w)

        def _quant_act(x):
            scale = 127.0 / jnp.clip(jnp.max(jnp.abs(x), axis=-1, keepdims=True), EPS, None)
            xq = jnp.clip(jnp.round(x * scale), -128.0, 127.0) / scale
            return x + jax.lax.stop_gradient(xq - x)

        def _bitlinear(x, w):
            return jnp.einsum('bsi,oi->bso', _quant_act(x), _quant_weight(w))
        key = jax.random.key(seed)
        k1, k2, k3 = jax.random.split(key, 3)
        x = jax.random.normal(k1, (BATCH, SEQ, EMBED_DIM), dtype=jnp.float32)
        w1 = jax.random.normal(k2, (HIDDEN, EMBED_DIM), dtype=jnp.float32) * (1.0 / np.sqrt(EMBED_DIM))
        w2 = jax.random.normal(k3, (EMBED_DIM, HIDDEN), dtype=jnp.float32) * (1.0 / np.sqrt(HIDDEN))
        return {'x': x, 'w1': w1, 'w2': w2}
    _L1_ffn_all = _L1_ffn_setup()
    _L1_ffn_in = {k: v for k, v in _L1_ffn_all.items() if k in ('w1', 'w2')}
    del _L1_ffn_all
    return {'x': x, 'ctx_1024': ctx_1024, 'g_xattn': g_xattn, 'g_ffn': g_ffn, 'L0_xattn_Wq': _L0_xattn_in['Wq'], 'L0_xattn_bq': _L0_xattn_in['bq'], 'L0_xattn_Wk': _L0_xattn_in['Wk'], 'L0_xattn_bk': _L0_xattn_in['bk'], 'L0_xattn_Wv': _L0_xattn_in['Wv'], 'L0_xattn_bv': _L0_xattn_in['bv'], 'L0_xattn_Wo': _L0_xattn_in['Wo'], 'L0_xattn_bo': _L0_xattn_in['bo'], 'L0_ffn_router_w': _L0_ffn_in['router_w'], 'L0_ffn_router_b': _L0_ffn_in['router_b'], 'L0_ffn_expert_weights': _L0_ffn_in['expert_weights'], 'L1_xattn_Wq': _L1_xattn_in['Wq'], 'L1_xattn_bq': _L1_xattn_in['bq'], 'L1_xattn_Wk': _L1_xattn_in['Wk'], 'L1_xattn_bk': _L1_xattn_in['bk'], 'L1_xattn_Wv': _L1_xattn_in['Wv'], 'L1_xattn_bv': _L1_xattn_in['bv'], 'L1_xattn_Wo': _L1_xattn_in['Wo'], 'L1_xattn_bo': _L1_xattn_in['bo'], 'L1_ffn_w1': _L1_ffn_in['w1'], 'L1_ffn_w2': _L1_ffn_in['w2']}

def reference(x, ctx_1024, g_xattn, g_ffn, L0_xattn_Wq, L0_xattn_bq, L0_xattn_Wk, L0_xattn_bk, L0_xattn_Wv, L0_xattn_bv, L0_xattn_Wo, L0_xattn_bo, L0_ffn_router_w, L0_ffn_router_b, L0_ffn_expert_weights, L1_xattn_Wq, L1_xattn_bq, L1_xattn_Wk, L1_xattn_bk, L1_xattn_Wv, L1_xattn_bv, L1_xattn_Wo, L1_xattn_bo, L1_ffn_w1, L1_ffn_w2):
    import jax
    import jax.numpy as jnp

    def _L0_xattn_ref(query, key, value, Wq, bq, Wk, bk, Wv, bv, Wo, bo):
        import jax, jax.numpy as jnp
        import numpy as np
        NUM_HEADS = 16
        DIM_MODEL = 256
        DIM_HEAD = DIM_MODEL // NUM_HEADS

        def _split_heads(x, B):
            return x.reshape(B, -1, NUM_HEADS, DIM_HEAD).transpose(0, 2, 1, 3)
        B = query.shape[0]
        q = _split_heads(query @ Wq.T + bq, B)
        k = _split_heads(key @ Wk.T + bk, B)
        v = _split_heads(value @ Wv.T + bv, B)
        inv_sqrt_d = 1.0 / jnp.sqrt(jnp.asarray(DIM_HEAD, q.dtype))
        scores = jnp.einsum('bhqd,bhkd->bhqk', q, k) * inv_sqrt_d
        weights = jax.nn.softmax(scores, axis=-1)
        out = jnp.einsum('bhqk,bhkd->bhqd', weights, v)
        out = out.transpose(0, 2, 1, 3).reshape(B, -1, NUM_HEADS * DIM_HEAD)
        return out @ Wo.T + bo

    def _L0_ffn_ref(tokens, router_w, router_b, expert_weights):
        import jax, jax.numpy as jnp
        import numpy as np
        TOP_K = 2
        EPS = 1e-10
        B, S, H = tokens.shape
        E = expert_weights.shape[0]
        logits = jnp.einsum('bsh,eh->bse', tokens, router_w) + router_b
        probs = jax.nn.softmax(logits, axis=-1)
        top_p, top_i = jax.lax.top_k(probs, TOP_K)
        w = top_p / (jnp.sum(top_p, axis=-1, keepdims=True) + EPS)
        x = tokens.reshape(-1, H)
        idx = top_i.reshape(-1, TOP_K)
        wf = w.reshape(-1, TOP_K)
        y_all = jnp.einsum('nh,ehd->ned', x, expert_weights)
        y_k = jnp.take_along_axis(y_all, idx[:, :, None], axis=1)
        out = jnp.einsum('nk,nkh->nh', wf, y_k)
        acc = jnp.clip(jnp.sum(wf, axis=-1), EPS, None)
        out = (out / acc[:, None]).reshape(B, S, H)
        scale = 1.0 + jnp.sum(w, axis=-1, keepdims=True) * EPS
        return out * scale

    def _L1_xattn_ref(query, key, value, Wq, bq, Wk, bk, Wv, bv, Wo, bo):
        import jax, jax.numpy as jnp
        import numpy as np
        D_MODEL = 256
        H = 16
        D_K = D_MODEL // H
        B, Sq, _ = query.shape

        def proj(x, W, b):
            y = x @ W.T + b
            return y.reshape(B, -1, H, D_K).transpose(0, 2, 1, 3)
        q = proj(query, Wq, bq)
        k = proj(key, Wk, bk)
        v = proj(value, Wv, bv)
        scores = jnp.einsum('bhqd,bhkd->bhqk', q, k) / jnp.sqrt(jnp.float32(D_K))
        attn = jax.nn.softmax(scores, axis=-1)
        ctx = jnp.einsum('bhqk,bhkd->bhqd', attn, v)
        ctx = ctx.transpose(0, 2, 1, 3).reshape(B, Sq, D_MODEL)
        return ctx @ Wo.T + bo

    def _L1_ffn_ref(x, w1, w2):
        import jax, jax.numpy as jnp
        import numpy as np
        EMBED_DIM = 256
        HIDDEN = 4 * EMBED_DIM
        BATCH, SEQ = (4, 1024)
        EPS = 1e-05

        def _quant_weight(w):
            s = jnp.clip(jnp.mean(jnp.abs(w)), EPS, None)
            wq = jnp.clip(jnp.round(w / s), -1.0, 1.0) * s
            return w + jax.lax.stop_gradient(wq - w)

        def _quant_act(x):
            scale = 127.0 / jnp.clip(jnp.max(jnp.abs(x), axis=-1, keepdims=True), EPS, None)
            xq = jnp.clip(jnp.round(x * scale), -128.0, 127.0) / scale
            return x + jax.lax.stop_gradient(xq - x)

        def _bitlinear(x, w):
            return jnp.einsum('bsi,oi->bso', _quant_act(x), _quant_weight(w))
        h = jax.nn.gelu(_bitlinear(x, w1), approximate=False)
        return _bitlinear(h, w2)
    x = x + jnp.tanh(g_xattn[0]) * _L0_xattn_ref(_layernorm(x, axis=-1), ctx_1024, ctx_1024, L0_xattn_Wq, L0_xattn_bq, L0_xattn_Wk, L0_xattn_bk, L0_xattn_Wv, L0_xattn_bv, L0_xattn_Wo, L0_xattn_bo)
    x = x + jnp.tanh(g_ffn[0]) * _L0_ffn_ref(_layernorm(x, axis=-1), L0_ffn_router_w, L0_ffn_router_b, L0_ffn_expert_weights)
    x = x + jnp.tanh(g_xattn[1]) * _L1_xattn_ref(_layernorm(x, axis=-1), ctx_1024, ctx_1024, L1_xattn_Wq, L1_xattn_bq, L1_xattn_Wk, L1_xattn_bk, L1_xattn_Wv, L1_xattn_bv, L1_xattn_Wo, L1_xattn_bo)
    x = x + jnp.tanh(g_ffn[1]) * _L1_ffn_ref(_layernorm(x, axis=-1), L1_ffn_w1, L1_ffn_w2)
    return x

_drawn_inputs = setup_inputs


def setup_inputs(seed=0):
    import zlib

    import numpy as np

    out = dict(_drawn_inputs(seed))
    spreads = {'g_ffn': (-1.0, 0.6),
     'L1_xattn_bq': (0.0, 0.506),
     'L1_xattn_bk': (0.0, 0.8),
     'L1_xattn_bv': (0.0, 0.1),
     'L1_xattn_bo': (0.0, 0.1)}
    factors = {'L0_xattn_bk': 8.0}
    for name, (base, spread) in spreads.items():
        noise = np.random.default_rng([zlib.crc32(name.encode()), seed]).standard_normal(out[name].shape)
        drawn = base * np.exp(spread * noise) if base else spread * noise
        out[name] = jnp.asarray(drawn.astype(out[name].dtype))
    for name, factor in factors.items():
        out[name] = (out[name] * factor).astype(out[name].dtype)
    return out
```

```python
from contextlib import ExitStack

import concourse.bass as bass
from concourse import mybir

F32 = mybir.dt.float32
BF16 = mybir.dt.bfloat16
U32 = mybir.dt.uint32
ALU = mybir.AluOpType
ACT = mybir.ActivationFunctionType
AX = mybir.AxisListType
RADD = bass.bass_isa.ReduceOp.add

P = 128
B, S, D = 4, 512, 256
H, DH = 16, 16
L = 2
NP = L * B
NT = S // P
NC = D // P
NE = 8
HID = 4 * D
GH = 4
NG = H // GH
SLOTS = 6
KR = DH * SLOTS
MP = 3
LEAD = 6
RING = 4
LN_EPS = 1e-5
MOE_EPS = 1e-10
Q_EPS = 1e-5
MAGIC = 12582912.0
SCALE = DH ** -0.5


class Count:

    def __init__(self):
        self.n, self.i, self.per = {}, None, {}

    def __call__(self, kind, mult=1, add=0):
        v = mult * self.n.get(kind, 0) + add
        d = mult * self.per.get(kind, 0)
        if self.i is None or d == 0:
            return max(v, 0) + 1
        assert v >= 0, (kind, v)
        return self.i * d + (v + 1)

    def index(self, kind, add=0):
        v, d = self.n.get(kind, 0) + add, self.per.get(kind, 0)
        return v if self.i is None or d == 0 else self.i * d + v

    def turn(self, kind):
        return self.n.get(kind, 0) % 2

    def add(self, kind, k=1):
        self.n[kind] = self.n.get(kind, 0) + k



def phase0_steps():
    out = [("LOAD0", ()), ("LN", (0,))]
    for l in range(L):
        for c in range(NC):
            out.append(("SPLIT", ("K", l, c)))
        for k in range(NT // 2):
            out.append(("VV", (l, k)))
        out.append(("VST", (l,)))
    for c in range(NC):
        out.append(("XT", (c,)))
    for c in range(NC):
        out.append(("SPLIT", ("Q", 0, c)))
    return out


def post0_steps():
    at = {u: [] for u in range(H)}
    at[0] += [("XLOAD", (0,))]
    at[2] += [("OT", (c,)) for c in range(NC)] + [("OP", (0, k)) for k in range(NT // 2)]
    at[3] += [("LN", (1,))]
    at[4] += [("XT", (c,)) for c in range(NC)]
    at[5] += [("RT", ())]
    for n in range(NT * NE // 2):
        at[5 + n // 2] += [("ME", (n // (NE // 2), n % (NE // 2)))]
    at[13] += [("XSTORE", (0,)), ("LN", (1,))]
    at[14] += [("XT", (c,)) for c in range(NC)]
    at[15] += [("SPLIT", ("Q", 1, c)) for c in range(NC)]
    return at


def post1_steps():
    at = {u: [] for u in range(H)}
    at[0] += [("XLOAD", (1,))]
    at[2] += [("OT", (c,)) for c in range(NC)] + [("OP", (1, k)) for k in range(NT // 2)]
    at[3] += [("LN", (1,)), ("XQ", ())]
    at[4] += [("XB", ())]
    at[6] += [("F1", (t, k)) for t in range(NT) for k in range(HID // 512)]
    for t in range(NT):
        at[8 + t] += [("HQ", (t,))]
        at[9 + t] += [("HT", (t,)), ("F2", (t,))]
    at[14] += [("XSTORE", (1,))]
    return at


def period_steps(first, last, post):
    out = [("PERIOD", ())]
    for u in range(H):
        lead = not last or u + LEAD < H
        pv = not (first and u == 0)
        out.append(("HEAD", (u, lead, pv)))
        if u % GH == 0:
            if pv:
                out.append(("OE", ()))
            if u > 0 and not last:
                out.append(("RELOAD", (u // GH - 1, 1)))
            if u == 0 and not first:
                out.append(("RELOAD", (NG - 1, 0)))
        if u % GH == 1 and not (first and u == 1):
            out.append(("NT", ((u // GH - 1) % NG,)))
        if (u + LEAD) % GH == GH - 1 and lead:
            out.append(("M", ()))
        if (u + LEAD) % GH == 0 and (not last or u + LEAD <= H):
            out.append(("MT", (((u + LEAD) // GH - 1) % NG,)))
        out += post[u] if post else []
    return out


def adds(kind, args):
    if kind == "HEAD":
        return [("S", int(args[1])), ("T", 1), ("PV", int(args[2]))]
    if kind in ("LEAD", "LASTPV"):
        return [("S" if kind == "LEAD" else "PV", 1)]
    return [(kind, 1)]


def walk(steps, ops, n):
    for kind, args in steps:
        if kind in ops:
            ops[kind](*args)
        for k, v in adds(kind, args):
            n.add(k, v)


def loop(eng, times, steps, ops, n):
    n.per = {}
    for kind, args in steps:
        for k, v in adds(kind, args):
            n.per[k] = n.per.get(k, 0) + v
    with eng.Fori(0, times) as i:
        n.i = i
        walk(steps, ops, n)
    for k, v in n.per.items():
        n.add(k, v * (times - 1))
    n.i, n.per = None, {}


def program(eng, ops, n):
    ops.get("INIT", lambda: None)()
    walk(phase0_steps(), ops, n)
    loop(eng, B - 1, phase0_steps(), ops, n)
    ops.get("PREP", lambda: None)()
    walk([("RELOAD", (g, 0)) for g in range(NG)], ops, n)
    walk([("LEAD", (u,)) for u in range(GH)], ops, n)
    walk([("M", ()), ("MT", (0,))], ops, n)
    walk([("LEAD", (u,)) for u in range(GH, LEAD)], ops, n)
    walk(period_steps(True, False, None), ops, n)
    loop(eng, B - 1, period_steps(False, False, post0_steps()), ops, n)
    walk(period_steps(False, False, post0_steps()), ops, n)
    loop(eng, B - 2, period_steps(False, False, post1_steps()), ops, n)
    walk(period_steps(False, True, post1_steps()), ops, n)
    walk([("PERIOD", ()), ("LASTPV", ()), ("OE", ()), ("NT", (NG - 1,))], ops, n)
    post = post1_steps()
    walk([s for u in range(H) for s in post[u]], ops, n)


def build(nc, x, ctxT, g_xattn, g_ffn, Wq, bq, Wk, bk, Wv, bv, Wo, bo, rw, rb, ew, w1, w2, out):
    with ExitStack() as ctx:
        def sb(name, shape, dt=F32):
            return ctx.enter_context(nc.sbuf_tensor(name, shape, dt))

        def ps(name, shape, dt=F32):
            return ctx.enter_context(nc.psum_tensor(name, shape, dt))

        def sem(name):
            return ctx.enter_context(nc.semaphore(name))

        kd = nc.dram_tensor("kd", [NP, NC, P, SLOTS, S], BF16, kind="Internal").ap()
        qd = nc.dram_tensor("qd", [NP, NC, P, SLOTS, S], BF16, kind="Internal").ap()
        vd = nc.dram_tensor("vd", [NP, NT, P, H * 32], F32, kind="Internal").ap()
        x2d = nc.dram_tensor("x2d", [B, S, D], F32, kind="Internal").ap()

        wq = [sb(f"wq{l}", [P, NC, D]) for l in range(L)]
        wk = [sb(f"wk{l}", [P, NC, D]) for l in range(L)]
        wv = [sb(f"wv{l}", [P, NC, D]) for l in range(L)]
        wo = [sb(f"wo{l}", [P, NC, D]) for l in range(L)]
        bqc = sb("bqc", [P, L, NC])
        bkc = sb("bkc", [P, L, NC])
        bvb = sb("bvb", [P, L, D])
        bob = sb("bob", [P, L, D])
        rwt = sb("rwt", [P, NC, NE])
        rbb = sb("rbb", [P, NE])
        moe = sb("moe", [P, NC, NE * D])
        w1q = sb("w1q", [P, NC, HID], BF16)
        w2q = sb("w2q", [P, HID // P, D], BF16)
        gate = sb("gate", [P, 4])
        gt = sb("gt", [P, 4])
        wsum = sb("wsum", [P, 2])
        wtot = sb("wtot", [P, 2])
        wmean = sb("wmean", [P, 2])
        wth = sb("wth", [P, 4])
        dqf = sb("dqf", [P, 2])
        identf = sb("identf", [P, P])
        identb = sb("identb", [P, P], BF16)
        halfs = sb("halfs", [P, NT])
        iota8 = sb("iota8", [P, NE])

        qs = sb("qs", [P, H, S], BF16)
        ks = sb("ks", [P, H, S], BF16)
        vg = sb("vg", [P, NT, H, 32])
        pt = sb("pt", [P, RING, NT, S])
        mx = sb("mx", [P, 2, GH * NT])
        mr = sb("mr", [P, 2, GH * NT])
        mp = sb("mp", [P, 2, P], BF16)
        mt = sb("mt", [MP * GH * NT, 2, P], BF16)
        osb = sb("osb", [P, 2, S])
        rinv = sb("rinv", [P, NT, GH])
        on = sb("on", [P, NT, D])
        ont = sb("ont", [P, NC, S])

        xin = sb("xin", [P, NT, D])
        x1 = sb("x1", [P, NT, D])
        xn = sb("xn", [P, NT, D])
        xnt = sb("xnt", [P, NC, S])
        st = sb("st", [P, NT, 6])
        mv = sb("mv", [P, NT, 2])
        lnw = sb("lnw", [P, 4, NT])
        ctxb = sb("ctxb", [P, NC, S])
        qf = sb("qf", [P, 2, S])
        qt = sb("qt", [P, 2, S])
        parts = sb("parts", [P, 2, 3, S], BF16)
        vst = sb("vst", [P, NT, H, 32])
        rt = sb("rt", [P, 10, NT, NE])
        rsm = sb("rsm", [P, 12, NT])
        ridx = sb("ridx", [P, NT, 8], U32)
        ridf = sb("ridf", [P, NT, 2])
        rw2 = sb("rw2", [P, NT, 2])
        coef = sb("coef", [P, NT, NE])
        hh = sb("hh", [P, NT, HID])
        hr = sb("hr", [P, HID])
        hq = sb("hq", [P, 2, HID], BF16)
        hqt = sb("hqt", [P, 2, HID // P, P], BF16)
        xi = sb("xi", [P, NT, D], BF16)
        xit = sb("xit", [P, NC, S], BF16)
        am = sb("am", [P, 6, NT])

        psS = ps("psS", [P, 2, S])
        psT = ps("psT", [P, 2, S])
        psO = ps("psO", [P, S])
        psA = ps("psA", [P, S])
        psX = ps("psX", [P, 2, S])

        c_load = sem("c_load")
        c_late = sem("c_late")
        c_pool = sem("c_pool")
        c_gate = sem("c_gate")
        c_prep = sem("c_prep")
        c_wabs = sem("c_wabs")
        c_wsum = sem("c_wsum")
        d_ctx = sem("d_ctx")
        d_x0 = sem("d_x0")
        d_xin = sem("d_xin")
        d_xst = sem("d_xst")
        pe_s = sem("pe_s")
        pe_t = sem("pe_t")
        pe_pv = sem("pe_pv")
        pe_mt = sem("pe_mt")
        pe_nt = sem("pe_nt")
        pe_SPLIT = sem("pe_SPLIT")
        pe_VV = sem("pe_VV")
        pe_XT = sem("pe_XT")
        pe_OT = sem("pe_OT")
        pe_OP = sem("pe_OP")
        pe_RT = sem("pe_RT")
        pe_ME = sem("pe_ME")
        pe_XB = sem("pe_XB")
        pe_F1 = sem("pe_F1")
        pe_HT = sem("pe_HT")
        pe_F2 = sem("pe_F2")
        a_exp = sem("a_exp")
        a_oe = sem("a_oe")
        a_mt = sem("a_mt")
        a_SPLIT = sem("a_SPLIT")
        a_XT = sem("a_XT")
        a_OT = sem("a_OT")
        a_rexp = sem("a_rexp")
        a_XB = sem("a_XB")
        a_F1 = sem("a_F1")
        a_HT = sem("a_HT")
        v_hr = sem("v_hr")
        v_prep = sem("v_prep")
        v_max = sem("v_max")
        v_norm = sem("v_norm")
        v_split = sem("v_split")
        v_VV = sem("v_VV")
        v_ln = sem("v_ln")
        v_OP = sem("v_OP")
        v_rt = sem("v_rt")
        v_ME = sem("v_ME")
        v_xq = sem("v_xq")
        v_hq = sem("v_hq")
        v_F2 = sem("v_F2")
        p_m = sem("p_m")
        p_ln = sem("p_ln")
        p_xb = sem("p_xb")
        d_p = [sem(f"d_p{r}") for r in range(2)]
        d_v = [sem(f"d_v{l}") for l in range(L)]
        d_m = [sem(f"d_m{r}") for r in range(2)]
        dq = [sem(f"d_q{g}") for g in range(NG)]
        dk = [sem(f"d_k{g}") for g in range(NG)]
        dv = [sem(f"d_v_{g}") for g in range(NG)]

        def apart(eng, sm, v):
            if not isinstance(v, int):
                v = eng.to_reg(v)
                eng.wait_ge(c_pool, 1)
            return sm, v

        N_LOADS = 18
        N_LATE = 6
        RT_OPS = 30
        LN_OPS = 3 * NT
        XQ_OPS = 11
        HQ_OPS = 6

        block = ctx.enter_context(nc.Block())

        @block.sync
        def _(sp):
            n = Count()

            def init():
                for one in (d_xin, d_xst, *d_p, *d_v, *d_m, *dq, *dk, *dv):
                    sp.sem_inc(one, 1)
                def load(dst, src, sm=c_load):
                    sp.dma_start(dst, src).then_inc(sm, 16)

                def rows(v, w):
                    return v.rearrange("(a n) -> a n", a=1).to_broadcast([P, w])

                for w, d in ((wk, Wk), (wv, Wv), (wq, Wq)):
                    for l in range(L):
                        load(w[l][:], d[l].rearrange("(c p) o -> p c o", p=P))
                for l in range(L):
                    load(bqc[:, l, :], bq[l])
                    load(bkc[:, l, :], bk[l])
                    load(bvb[:, l, :], rows(bv[l], D))
                    load(bob[:, l, :], rows(bo[l], D))
                load(gate[:, 0:2], rows(g_xattn, 2))
                load(gate[:, 2:4], rows(g_ffn, 2))
                load(rwt[:], rw.rearrange("(c p) o -> p c o", p=P))
                load(rbb[:], rows(rb, NE))
                load(hh[:, 0:2, :], w1.rearrange("(c p) o -> p c o", p=P), c_late)
                load(hh[:, 2:4, :].rearrange("p a (b o) -> p (a b) o", o=D), w2.rearrange("(c p) o -> p c o", p=P),
                     c_late)
                for l in range(L):
                    load(wo[l][:], Wo[l].rearrange("(c p) o -> p c o", p=P), c_late)
                for c in range(NC):
                    load(moe[:, c, :], ew[c * P:(c + 1) * P, :], c_late)

            def batch(l):
                return n.index("LOAD0", l * B - 1)

            def split(what, l, c):
                r = n.turn("SPLIT")
                sp.wait_ge(*apart(sp, v_split, n("SPLIT", 3, 3)))
                if what == "K" or l == 0:
                    at = (kd if what == "K" else qd)[batch(l)]
                else:
                    at = qd[n.index("XLOAD", B - 1)]
                pr = parts[:, r]
                if what == "Q":
                    sp.dma_start(at[c, :, 0:3, :], pr[:, 0:3, :]).then_inc(d_p[r], 16)
                    sp.dma_start(at[c, :, 3:5, :], pr[:, 0:2, :]).then_inc(d_p[r], 16)
                    sp.dma_start(at[c, :, 5, :], pr[:, 0, :]).then_inc(d_p[r], 16)
                else:
                    sp.dma_start(at[c, :, 0:3, :], pr[:, 0:1, :].to_broadcast([P, 3, S])).then_inc(d_p[r], 16)
                    sp.dma_start(at[c, :, 3:5, :], pr[:, 1:2, :].to_broadcast([P, 2, S])).then_inc(d_p[r], 16)
                    sp.dma_start(at[c, :, 5, :], pr[:, 2, :]).then_inc(d_p[r], 16)

            def vstore(l):
                sp.wait_ge(*apart(sp, v_VV, n("VV")))
                sp.dma_start(vd[batch(l)].rearrange("k p f -> p k f"),
                             vst[:].rearrange("p k h f -> p k (h f)")).then_inc(d_v[l], 16)

            def reload(g, ahead):
                for r in range(2):
                    sp.wait_ge(*apart(sp, d_p[r], n("SPLIT", 24)))
                for l in range(L):
                    sp.wait_ge(*apart(sp, d_v[l], n("VST", 8)))
                p = n.index("PERIOD", ahead - 1) if "PERIOD" in n.n else 0
                sp.wait_ge(*apart(sp, pe_t, n("T", 4, -4)))
                c, r0 = g // 2, g % 2 * GH * DH
                for stack, dram, sm in ((qs, qd, dq), (ks, kd, dk)):
                    sp.dma_start(stack[0:KR, g * GH:(g + 1) * GH, :],
                                 dram[p, c, r0:r0 + GH * DH].rearrange("(h d) s t -> (d s) h t", h=GH)
                                 ).then_inc(sm[g], 16)
                sp.wait_ge(*apart(sp, pe_pv, n("PV", 4)))
                sp.dma_start(vg[:, :, g * GH:(g + 1) * GH, :].rearrange("p k h f -> p k (h f)"),
                             vd[p, :, :, g * GH * 32:(g + 1) * GH * 32].rearrange("k p f -> p k f")
                             ).then_inc(dv[g], 16)

            def max_rows(g):
                r = n.turn("MT")
                sp.wait_ge(*apart(sp, a_mt, n("MT", 1, 1)))
                for k in range(MP):
                    sp.dma_start(qs[KR + k:KR + k + 1, g * GH:(g + 1) * GH, :].rearrange("p h (t q) -> p (h t) q", q=P),
                                 mt[k * GH * NT:(k + 1) * GH * NT, r, :]).then_inc(d_m[r], 16)

            def xload(l):
                sp.wait_ge(*apart(sp, p_xb, n("XLOAD")))
                sp.wait_ge(v_ln, B * LN_OPS + 1)
                if l:
                    sp.wait_ge(d_xst, 16 * B + 1)
                b = n.index("XLOAD", -l * B)
                src = x if l == 0 else x2d
                sp.dma_start(xin[:], src[b].rearrange("(t p) d -> p t d", p=P)).then_inc(d_xin, 16)

            def xstore(l):
                b = n.index("XSTORE", -l * B)
                if l == 0:
                    sp.wait_ge(*apart(sp, v_ME, n("ME", 2)))
                    sp.dma_start(x2d[b].rearrange("(t p) d -> p t d", p=P), x1[:]).then_inc(d_xst, 16)
                else:
                    sp.wait_ge(*apart(sp, v_F2, n("F2")))
                    sp.dma_start(out[b].rearrange("(t p) d -> p t d", p=P), x1[:]).then_inc(d_xst, 16)

            program(sp, {"INIT": init, "SPLIT": split, "VST": vstore, "RELOAD": reload, "MT": max_rows,
                         "XLOAD": xload, "XSTORE": xstore}, n)
            sp.wait_ge(*apart(sp, d_xst, n("XSTORE", 16)))
            for r in range(2):
                sp.wait_ge(*apart(sp, d_p[r], n("SPLIT", 24)))
            for l in range(L):
                sp.wait_ge(*apart(sp, d_v[l], n("VST", 8)))

        @block.gpsimd
        def _(pool):
            n = Count()
            g = nc.gpsimd

            def init():
                for one in (p_m, p_ln, p_xb):
                    pool.sem_inc(one, 1)
                for k, (dst, v) in enumerate(((identf[:], 0.0), (identb[:], 0.0), (halfs[:], -0.5), (mp[:], 0.0),
                                              (vst[:], 1.0), (ks[KR:KR + MP], -1.0))):
                    if k == 5:
                        pool.wait_ge(c_pool, 5)
                    g.memset(dst, v).then_inc(c_pool, 1)
                pool.wait_ge(c_pool, 6)
                g.iota(iota8[:], pattern=[[1, NE]], base=0, channel_multiplier=0,
                       allow_small_or_imprecise_dtypes=True).then_inc(c_pool, 1)
                pool.wait_ge(c_pool, 7)
                for m in (identf, identb):
                    g.affine_select(out=m[:], in_=m[:], compare_op=ALU.not_equal, fill=1.0, base=0,
                                    pattern=[[-1, P]], channel_multiplier=1).then_inc(c_pool, 1)

            def load0():
                b = n.index("LOAD0")
                pool.wait_ge(*apart(pool, v_ln, n("LN", LN_OPS)))
                pool.dma_start(xin[:], x[b].rearrange("(t p) d -> p t d", p=P)).then_inc(d_x0, 16)
                pool.wait_ge(*apart(pool, pe_VV, n("VV")))
                pool.dma_start(ctxb[:], ctxT[b].rearrange("(c p) t -> p c t", p=P)).then_inc(d_ctx, 16)

            def ln(src):
                pool.wait_ge(*apart(pool, v_ln, n("LN", LN_OPS, 2 * NT)))
                ve, r0, t0, r1 = (lnw[:, k, :] for k in range(4))
                steps = [lambda: g.tensor_scalar(ve, mv[:, :, 1], LN_EPS, None, ALU.add),
                         lambda: g.tensor_tensor(r0, ve, halfs[:], ALU.pow),
                         lambda: g.tensor_tensor(t0, r0, r0, ALU.mult),
                         lambda: g.tensor_tensor(t0, t0, ve, ALU.mult),
                         lambda: g.tensor_scalar(t0, t0, -0.5, 1.5, ALU.mult, ALU.add),
                         lambda: g.tensor_tensor(r1, r0, t0, ALU.mult)]
                for k, f in enumerate(steps):
                    f().then_inc(p_ln, 1)
                    pool.wait_ge(*apart(pool, p_ln, n("LN", 6, k + 1)))

            def prep():
                pool.wait_ge(c_wabs, 2)
                g.partition_all_reduce(wtot[:], wsum[:], P, RADD).then_inc(c_wsum, 1)

            def m():
                r = n.turn("M")
                pool.wait_ge(*apart(pool, v_max, n("M", 4 * GH, 4 * GH)))
                pool.wait_ge(*apart(pool, pe_mt, n("M", 1, -1)))
                w = GH * NT
                p1, p2, p3 = (mp[:, r, k * w:(k + 1) * w] for k in range(MP))
                steps = [lambda: g.tensor_copy(p1, mx[:, r]),
                         lambda: g.tensor_tensor(mr[:, r], mx[:, r], p1, ALU.subtract),
                         lambda: g.tensor_copy(p2, mr[:, r]),
                         lambda: g.tensor_tensor(p3, mr[:, r], p2, ALU.subtract)]
                for k, f in enumerate(steps):
                    f().then_inc(p_m, 1)
                    pool.wait_ge(*apart(pool, p_m, n("M", 4, k + 1)))

            def xb(l):
                pool.wait_ge(*apart(pool, d_xin, n("XLOAD", 16, 16)))
                pool.wait_ge(*apart(pool, c_prep, 4))
                pool.wait_ge(*apart(pool, d_xst, n("XSTORE", 16)))
                pool.wait_ge(*apart(pool, v_ln, n("LN", LN_OPS)))
                g.tensor_tensor(x1[:], xin[:], bob[:, l:l + 1, :].to_broadcast([P, NT, D]), ALU.add
                                ).then_inc(p_xb, 1)

            program(pool, {"INIT": init, "LOAD0": load0, "LN": ln, "PREP": prep, "M": m, "XLOAD": xb}, n)

        @block.tensor
        def _(pe):
            n = Count()
            mm = nc.tensor.matmul
            freed = {"VV": (v_VV, 1, 1), "SPLIT": (a_SPLIT, 2, 2), "XT": (a_XT, 1, 1), "OT": (a_OT, 1, 1),
                     "OP": (v_OP, 1, 1), "RT": (v_rt, RT_OPS, 1), "ME": (v_ME, 2, 2), "XB": (a_XB, 1, 1),
                     "F1": (a_F1, 1, 1), "HT": (a_HT, 1, 1), "F2": (v_F2, 1, 1)}
            use = {"k": 0, "last": [None, None]}

            def reset():
                use["k"], use["last"] = 0, [None, None]

            def bank(kind):
                b = use["k"] % 2
                if use["last"][b] is None:
                    for k, (sm, per, _) in freed.items():
                        if n.n.get(k, 0) or n.per.get(k, 0):
                            pe.wait_ge(sm, n(k, per))
                else:
                    k, v = use["last"][b]
                    pe.wait_ge(freed[k][0], v)
                use["last"][b] = (kind, n(kind, freed[kind][1], freed[kind][2]))
                use["k"] += 1
                return psX[:, b, :]

            def init():
                for one in (pe_s, pe_t, pe_pv, pe_mt, pe_nt, pe_SPLIT, pe_VV, pe_XT, pe_OT,
                            pe_OP, pe_RT, pe_ME, pe_XB, pe_F1, pe_HT, pe_F2):
                    pe.sem_inc(one, 1)
                pe.wait_ge(c_pool, 9)
                pe.wait_ge(c_load, 16 * N_LOADS)

            def load0():
                reset()
                pe.wait_ge(d_ctx, n("LOAD0", 16, 15))

            def split(what, l, c):
                o = bank("SPLIT")
                if what == "Q":
                    pe.wait_ge(a_XT, n("XT"))
                w, src = (wk[l], ctxb) if what == "K" else (wq[l], xnt)
                for k in range(NC):
                    i = mm(o, w[:, k, c * P:(c + 1) * P], src[:, k, :], start=k == 0, stop=k == NC - 1)
                i.then_inc(pe_SPLIT, 1)

            def vv(l, half):
                o = bank("VV")
                for t in range(2):
                    for k in range(NC):
                        i = mm(o[:, t * D:(t + 1) * D], ctxb[:, k, (2 * half + t) * P:(2 * half + t + 1) * P],
                               wv[l][:, k, :], start=k == 0, stop=k == NC - 1)
                i.then_inc(pe_VV, 1)

            def xt(c):
                o = bank("XT")
                pe.wait_ge(v_ln, n("LN", LN_OPS))
                for t in range(NT):
                    i = nc.tensor.transpose(o[:, t * P:(t + 1) * P], xn[:, t, c * P:(c + 1) * P], identf[:])
                i.then_inc(pe_XT, 1)

            def s_tile(u, k, idx):
                h = u % H
                if k == 0 and h % GH == 0:
                    pe.wait_ge(dq[h // GH], idx)
                    pe.wait_ge(dk[h // GH], idx)
                pe.wait_ge(v_max, n("S", 4, k - 1))
                mm(psS[:, k % 2, :], qs[0:KR, h, k * P:(k + 1) * P], ks[0:KR, h, :], start=True, stop=True
                   ).then_inc(pe_s, 1)

            def t_tile(u, k):
                if k == 0 and u % GH == 0:
                    g = u // GH
                    r = g % 2
                    pe.wait_ge(d_m[r], n("PERIOD", 96, -96 + 48 * (g // 2 + 1)))
                pe.wait_ge(a_exp, n("T", 4, k - 1))
                mm(psT[:, k % 2, :], ks[0:KR + MP, u, k * P:(k + 1) * P], qs[0:KR + MP, u, :], start=True, stop=True
                   ).then_inc(pe_t, 1)

            def pv_tile(u, k):
                h = (u - 1) % H
                j = h % GH
                if k == 0 and j == 0:
                    pe.wait_ge(dv[h // GH], n("PERIOD", 16))
                    pe.wait_ge(a_oe, n("OE"))
                pe.wait_ge(a_exp, n("PV", 4, k + 1))
                mm(psO[32 * j:32 * j + 32, :], vg[:, k, h, :], pt[:, h % RING, k, :], start=k == 0, stop=k == NT - 1,
                   tile_position=(0, 32 * j)).then_inc(pe_pv, 1)

            def head(u, lead, pv):
                for k in range(NT):
                    if lead:
                        per = n("PERIOD", 16) if u + LEAD < H else n("PERIOD", 16, 16)
                        s_tile(u + LEAD, k, per)
                    t_tile(u, k)
                    if pv:
                        pv_tile(u, k)

            def m_transpose(g):
                pe.wait_ge(a_mt, n("MT"))
                pe.wait_ge(v_norm, n("NT", 2))
                pe.wait_ge(p_m, n("MT", 4, 4))
                nc.tensor.transpose(psA[:, 0:P // 2].bitcast(BF16), mp[:, n.turn("MT"), :],
                                    identb[:]).then_inc(pe_mt, 1)

            def o_transpose(g):
                pe.wait_ge(a_oe, n("NT", 1, 1))
                pe.wait_ge(a_mt, n("MT"))
                pe.wait_ge(v_norm, n("NT", 2))
                r = n.turn("NT")
                for t in range(NT):
                    i = nc.tensor.transpose(psA[:, t * P:(t + 1) * P], osb[:, r, t * P:(t + 1) * P], identf[:])
                i.then_inc(pe_nt, 1)

            def ot(c):
                o = bank("OT")
                pe.wait_ge(v_norm, n("NT", 2))
                for t in range(NT):
                    i = nc.tensor.transpose(o[:, t * P:(t + 1) * P], on[:, t, c * P:(c + 1) * P], identf[:])
                i.then_inc(pe_OT, 1)

            def op(l, half):
                o = bank("OP")
                pe.wait_ge(a_OT, n("OT"))
                for t in range(2):
                    for k in range(NC):
                        tt = 2 * half + t
                        i = mm(o[:, t * D:(t + 1) * D], ont[:, k, tt * P:(tt + 1) * P], wo[l][:, k, :],
                               start=k == 0, stop=k == NC - 1)
                i.then_inc(pe_OP, 1)

            def router():
                o = bank("RT")
                pe.wait_ge(a_XT, n("XT"))
                for t in range(NT):
                    for k in range(NC):
                        i = mm(o[:, t * NE:(t + 1) * NE], xnt[:, k, t * P:(t + 1) * P], rwt[:, k, :],
                               start=k == 0, stop=k == NC - 1)
                i.then_inc(pe_RT, 1)

            def experts(t, e2):
                o = bank("ME")
                for k in range(NC):
                    i = mm(o, xnt[:, k, t * P:(t + 1) * P], moe[:, k, e2 * S:(e2 + 1) * S],
                           start=k == 0, stop=k == NC - 1)
                i.then_inc(pe_ME, 1)

            def xb():
                o = bank("XB").bitcast(BF16)
                pe.wait_ge(c_prep, 4)
                pe.wait_ge(v_xq, n("XQ", XQ_OPS))
                for c in range(NC):
                    for t in range(NT):
                        i = nc.tensor.transpose(o[:, c * S + t * P:c * S + (t + 1) * P], xi[:, t, c * P:(c + 1) * P],
                                                identb[:])
                i.then_inc(pe_XB, 1)

            def f1(t, half):
                o = bank("F1")
                pe.wait_ge(a_XB, n("XB"))
                for k in range(NC):
                    i = mm(o, xit[:, k, t * P:(t + 1) * P], w1q[:, k, half * S:(half + 1) * S],
                           start=k == 0, stop=k == NC - 1)
                i.then_inc(pe_F1, 1)

            def ht(t):
                o = bank("HT").bitcast(BF16)
                pe.wait_ge(v_hq, n("HT", HQ_OPS, HQ_OPS))
                for k in range(HID // P):
                    i = nc.tensor.transpose(o[:, k * P:(k + 1) * P], hq[:, t % 2, k * P:(k + 1) * P], identb[:])
                i.then_inc(pe_HT, 1)

            def f2(t):
                o = bank("F2")
                pe.wait_ge(a_HT, n("HT"))
                for k in range(HID // P):
                    i = mm(o[:, 0:D], hqt[:, t % 2, k, :], w2q[:, k, :], start=k == 0, stop=k == HID // P - 1)
                i.then_inc(pe_F2, 1)

            def prep():
                pe.wait_ge(c_late, 16 * N_LATE)

            def lead(u):
                for k in range(NT):
                    s_tile(u, k, 17)

            def last_pv():
                for k in range(NT):
                    pv_tile(H, k)

            program(pe, {"INIT": init, "LOAD0": load0, "SPLIT": split, "VV": vv, "XT": xt, "PREP": prep,
                         "LEAD": lead, "PERIOD": reset, "HEAD": head, "LASTPV": last_pv, "MT": m_transpose,
                         "NT": o_transpose, "OT": ot, "OP": op, "RT": router, "ME": experts, "XB": xb, "F1": f1,
                         "HT": ht, "F2": f2}, n)

        @block.scalar
        def _(act):
            n = Count()
            a = nc.scalar.activation

            use = {"k": 0}

            def bank():
                b = use["k"] % 2
                use["k"] += 1
                return psX[:, b, :]

            def skip(*_):
                use["k"] += 1

            def reset():
                use["k"] = 0

            def init():
                for one in (a_exp, a_oe, a_mt, a_SPLIT, a_XT, a_OT, a_rexp, a_XB, a_F1, a_HT):
                    act.sem_inc(one, 1)
                act.wait_ge(c_load, 16 * N_LOADS)
                a(gt[:], gate[:], ACT.Tanh).then_inc(c_gate, 1)

            def split(what, l, c):
                o = bank()
                r = n.turn("SPLIT")
                bias = (bkc if what == "K" else bqc)[:, l, c:c + 1]
                act.wait_ge(pe_SPLIT, n("SPLIT", 1, 1))
                act.wait_ge(v_split, n("SPLIT", 3, -3))
                act.wait_ge(d_p[r], n("SPLIT", 24, -24 * r))
                a(qf[:, r, :], o, ACT.Identity, bias=bias).then_inc(a_SPLIT, 1)
                a(parts[:, r, 0, :], o, ACT.Identity, bias=bias).then_inc(a_SPLIT, 1)

            def xt(c):
                o = bank()
                act.wait_ge(pe_XT, n("XT", 1, 1))
                act.wait_ge(pe_SPLIT, n("SPLIT"))
                act.wait_ge(pe_ME, n("ME"))
                act.wait_ge(pe_RT, n("RT"))
                a(xnt[:, c, :], o, ACT.Copy).then_inc(a_XT, 1)

            def ot(c):
                o = bank()
                act.wait_ge(pe_OT, n("OT", 1, 1))
                act.wait_ge(pe_OP, n("OP"))
                a(ont[:, c, :], o, ACT.Copy).then_inc(a_OT, 1)

            def head(u, lead, pv):
                for k in range(NT):
                    if k == 0:
                        act.wait_ge(pe_pv, n("T", 4, -4 * (RING - 1)))
                    act.wait_ge(pe_t, n("T", 4, k + 1))
                    a(pt[:, u % RING, k, :], psT[:, k % 2, :], ACT.Exp, scale=SCALE).then_inc(a_exp, 1)

            def oe():
                act.wait_ge(pe_pv, n("OE", 4 * GH, 4 * GH))
                act.wait_ge(pe_nt, n("OE", 1, -1))
                a(osb[:, n.turn("OE"), :], psO[:], ACT.Copy).then_inc(a_oe, 1)

            def mt_(g):
                r = n.turn("MT")
                act.wait_ge(pe_mt, n("MT", 1, 1))
                act.wait_ge(d_m[r], n("MT", 24, -24 * r))
                a(mt[:, r, :], psA[0:MP * GH * NT, 0:P // 2].bitcast(BF16), ACT.Copy).then_inc(a_mt, 1)

            def router():
                skip()
                act.wait_ge(v_rt, n("RT", RT_OPS, 3))
                a(rt[:, 2], rt[:, 1], ACT.Exp).then_inc(a_rexp, 1)

            def xb():
                o = bank().bitcast(BF16)
                act.wait_ge(pe_XB, n("XB", 1, 1))
                act.wait_ge(pe_F1, n("F1"))
                a(xit[:].rearrange("p c t -> p (c t)"), o, ACT.Copy).then_inc(a_XB, 1)

            def f1(t, half):
                o = bank()
                act.wait_ge(pe_F1, n("F1", 1, 1))
                act.wait_ge(v_hq, n("HQ", HQ_OPS))
                act.wait_ge(c_prep, 4)
                a(hh[:, t, half * S:(half + 1) * S], o, ACT.Gelu, scale=am[:, 2, t:t + 1]).then_inc(a_F1, 1)

            def ht(t):
                o = bank().bitcast(BF16)
                act.wait_ge(pe_HT, n("HT", 1, 1))
                act.wait_ge(pe_F2, n("HT", 1, -min(t, 1)))
                a(hqt[:, t % 2].rearrange("p k t -> p (k t)"), o, ACT.Copy).then_inc(a_HT, 1)

            def prep():
                act.wait_ge(c_late, 16 * N_LATE)
                for k in range(2):
                    a(pt[:, k], hh[:, 2 * k:2 * k + 2, :].rearrange("p a (b f) -> p (a b) f", f=S), ACT.Abs,
                      accum_out=wsum[:, k:k + 1]).then_inc(c_wabs, 1)
                act.wait_ge(c_wabs, 2)

            program(act, {"INIT": init, "LOAD0": reset, "SPLIT": split, "VV": skip, "XT": xt, "PREP": prep,
                          "PERIOD": reset, "HEAD": head, "OE": oe, "MT": mt_, "OT": ot, "OP": skip, "RT": router,
                          "ME": skip, "XB": xb, "F1": f1, "HT": ht, "F2": skip}, n)

        @block.vector
        def _(dve):
            n = Count()
            v = nc.vector
            use = {"k": 0}

            def bank():
                b = use["k"] % 2
                use["k"] += 1
                return psX[:, b, :]

            def skip(*_):
                use["k"] += 1

            def reset():
                use["k"] = 0

            def init():
                for one in (v_hr, v_prep, v_max, v_norm, v_split, v_VV, v_ln, v_OP, v_rt,
                            v_ME, v_xq, v_hq, v_F2):
                    dve.sem_inc(one, 1)
                dve.wait_ge(c_load, 16 * N_LOADS)
                dve.wait_ge(c_pool, 9)
                dve.wait_ge(c_gate, 1)
                for l in range(L):
                    v.tensor_scalar(bob[:, l, :], bob[:, l, :], gt[:, l:l + 1], None, ALU.mult).then_inc(c_prep, 1)

            def ln(src):
                xs = x1 if src else xin
                dve.wait_ge(v_ln, n("LN", LN_OPS))
                dve.wait_ge(v_xq, n("XQ", XQ_OPS))
                if src:
                    dve.wait_ge(v_OP, n("OP"))
                    dve.wait_ge(v_ME, n("ME", 2))
                else:
                    dve.wait_ge(d_x0, n("LN", 16, 15))
                for t in range(NT):
                    v.bn_stats(st[:, t, :], xs[:, t, :]).then_inc(v_ln, 1)
                for t in range(NT):
                    dve.wait_ge(*apart(dve, v_ln, n("LN", LN_OPS, t + 1)))
                    v.bn_aggr(mv[:, t, :], st[:, t, :]).then_inc(v_ln, 1)
                dve.wait_ge(p_ln, n("LN", 6, 6))
                dve.wait_ge(pe_XT, n("XT"))
                for t in range(NT):
                    v.tensor_scalar(xn[:, t, :], xs[:, t, :], mv[:, t, 0:1], lnw[:, 3, t:t + 1], ALU.subtract,
                                    ALU.mult).then_inc(v_ln, 1)

            def split(what, l, c):
                skip()
                r = n.turn("SPLIT")
                dve.wait_ge(a_SPLIT, n("SPLIT", 2, 2))
                dve.wait_ge(v_split, n("SPLIT", 3))
                v.tensor_tensor(qt[:, r, :], qf[:, r, :], parts[:, r, 0, :], ALU.subtract).then_inc(v_split, 1)
                dve.wait_ge(v_split, n("SPLIT", 3, 1))
                v.tensor_copy(parts[:, r, 1, :], qt[:, r, :]).then_inc(v_split, 1)
                dve.wait_ge(v_split, n("SPLIT", 3, 2))
                v.tensor_tensor(parts[:, r, 2, :], qt[:, r, :], parts[:, r, 1, :], ALU.subtract).then_inc(v_split, 1)

            def vv(l, half):
                o = bank()
                dve.wait_ge(pe_VV, n("VV", 1, 1))
                dve.wait_ge(d_v[1 - l], n("VST", 8, 0) if l == 0 else n("VST", 8, 8))
                v.tensor_tensor(vst[:, 2 * half:2 * half + 2, :, 0:DH], o.rearrange("p (k h d) -> p k h d", k=2, d=DH),
                                bvb[:, l:l + 1, :].rearrange("p a (h d) -> p a h d", d=DH).to_broadcast([P, 2, H, DH]),
                                ALU.add).then_inc(v_VV, 1)

            def prep():
                dve.wait_ge(c_wsum, 1)
                v.tensor_scalar(wmean[:], wtot[:], 1.0 / (D * HID), Q_EPS, ALU.mult, ALU.max).then_inc(v_prep, 1)
                dve.wait_ge(v_prep, 2)
                v.tensor_scalar(wth[:, 0:2], wmean[:], 0.5, None, ALU.mult).then_inc(v_prep, 1)
                v.tensor_scalar(wth[:, 2:4], wmean[:], -0.5, None, ALU.mult).then_inc(v_prep, 1)
                v.tensor_scalar(dqf[:, 0:1], wmean[:, 0:1], 1.0 / 127.0, None, ALU.mult).then_inc(v_prep, 1)
                v.tensor_scalar(dqf[:, 1:2], wmean[:, 1:2], gt[:, 3:4], 1.0 / 127.0, ALU.mult, ALU.mult).then_inc(v_prep, 1)
                dve.wait_ge(v_prep, 6)
                for k, wt in enumerate((w1q, w2q)):
                    raw = hh[:, 2 * k:2 * k + 2, :].rearrange("p a b -> p (a b)")
                    flat = wt[:].rearrange("p a b -> p (a b)")
                    v.tensor_scalar(flat, raw, wth[:, 2 + k:3 + k], None, ALU.is_lt).then_inc(v_prep, 1)
                    dve.wait_ge(v_prep, 7 + k)
                    v.scalar_tensor_tensor(out=flat, in0=raw, scalar=wth[:, k:k + 1], in1=flat, op0=ALU.is_gt,
                                           op1=ALU.subtract).then_inc(c_prep, 1)
                dve.wait_ge(c_prep, 4)

            def maxima(u):
                h = n.n.get("S", 0)
                r, j = h // GH % 2, h % GH
                for k in range(NT):
                    if k == 0 and j == 0:
                        dve.wait_ge(p_m, n("M", 4, -4))
                    dve.wait_ge(pe_s, n("S", 4, k + 1))
                    v.tensor_reduce(mx[:, r, j * NT + k:j * NT + k + 1], psS[:, k % 2, :], AX.X, ALU.max
                                    ).then_inc(v_max, 1)

            def head(u, lead, pv):
                if lead:
                    maxima(u)

            def norm(g):
                dve.wait_ge(pe_nt, n("NT", 1, 1))
                o = psA[:].rearrange("p (t j f) -> p t j f", j=GH, f=32)
                dve.wait_ge(v_norm, n("NT", 2))
                v.reciprocal(rinv[:], o[:, :, :, DH]).then_inc(v_norm, 1)
                dve.wait_ge(v_norm, n("NT", 2, 1))
                if g == 0:
                    dve.wait_ge(pe_OT, n("OT"))
                v.tensor_tensor(on[:, :, g * GH * DH:(g + 1) * GH * DH].rearrange("p t (j d) -> p t j d", d=DH),
                                o[:, :, :, 0:DH], rinv[:].unsqueeze(3).to_broadcast([P, NT, GH, DH]), ALU.mult
                                ).then_inc(v_norm, 1)

            def op(l, half):
                o = bank()
                dve.wait_ge(pe_OP, n("OP", 1, 1))
                dve.wait_ge(p_xb, n("XLOAD"))
                xs = x1[:, 2 * half:2 * half + 2, :].rearrange("p t d -> p (t d)")
                v.scalar_tensor_tensor(out=xs, in0=o, scalar=gt[:, l:l + 1], in1=xs, op0=ALU.mult, op1=ALU.add
                                       ).then_inc(v_OP, 1)

            def router():
                o = bank()
                count = [0]

                def link(ins):
                    count[0] += 1
                    ins.then_inc(v_rt, 1)
                    dve.wait_ge(*apart(dve, v_rt, n("RT", RT_OPS, count[0])))

                dve.wait_ge(pe_RT, n("RT", 1, 1))
                dve.wait_ge(v_ME, n("ME", 2))
                lg, cent, ex, pr, top, e1, e2 = (rt[:, k] for k in range(7))
                mxl, sm, rs, tw, wr, acc, ra, sc = (rsm[:, k] for k in range(8))

                def bc(m):
                    return m.unsqueeze(2).to_broadcast([P, NT, NE])

                link(v.tensor_tensor(lg, o[:, 0:NT * NE].rearrange("p (t e) -> p t e", e=NE),
                                     rbb[:].unsqueeze(1).to_broadcast([P, NT, NE]), ALU.add))
                link(v.tensor_reduce(mxl, lg, AX.X, ALU.max))
                link(v.tensor_tensor(cent, lg, bc(mxl), ALU.subtract))
                dve.wait_ge(a_rexp, n("RT", 1, 1))
                link(v.tensor_reduce(sm, ex, AX.X, ALU.add))
                link(v.reciprocal(rs, sm))
                link(v.tensor_tensor(pr, ex, bc(rs), ALU.mult))
                for t in range(NT):
                    link(v.max(top[:, t], pr[:, t]))
                    link(v.max_index(ridx[:, t], top[:, t], pr[:, t]))
                link(v.tensor_copy(ridf[:], ridx[:, :, 0:2]))
                link(v.tensor_tensor(tw, top[:, :, 0], top[:, :, 1], ALU.add))
                link(v.tensor_scalar(tw, tw, MOE_EPS, None, ALU.add))
                link(v.reciprocal(wr, tw))
                link(v.tensor_tensor(rw2[:], top[:, :, 0:2], wr.unsqueeze(2).to_broadcast([P, NT, 2]), ALU.mult))
                link(v.tensor_tensor(acc, rw2[:, :, 0], rw2[:, :, 1], ALU.add))
                link(v.tensor_scalar(sc, acc, MOE_EPS, 1.0, ALU.mult, ALU.add))
                link(v.tensor_scalar(acc, acc, MOE_EPS, None, ALU.max))
                link(v.reciprocal(ra, acc))
                link(v.scalar_tensor_tensor(out=ra, in0=ra, scalar=gt[:, 2:3], in1=sc, op0=ALU.mult, op1=ALU.mult))
                link(v.tensor_tensor(rw2[:], rw2[:], ra.unsqueeze(2).to_broadcast([P, NT, 2]), ALU.mult))
                for k, e in enumerate((e1, e2)):
                    io = iota8[:].unsqueeze(1).to_broadcast([P, NT, NE])
                    link(v.tensor_tensor(e, io, ridf[:, :, k:k + 1].to_broadcast([P, NT, NE]), ALU.is_equal))
                    link(v.tensor_tensor(e, e, rw2[:, :, k:k + 1].to_broadcast([P, NT, NE]), ALU.mult))
                link(v.tensor_tensor(coef[:], e1, e2, ALU.add))
                assert count[0] == RT_OPS, count

            def experts(t, e2):
                o = bank()
                dve.wait_ge(pe_ME, n("ME", 1, 1))
                dve.wait_ge(v_ln, n("LN", LN_OPS))
                for k in range(2):
                    e = 2 * e2 + k
                    dve.wait_ge(v_ME, n("ME", 2, k))
                    v.scalar_tensor_tensor(out=x1[:, t, :], in0=o[:, k * D:(k + 1) * D], scalar=coef[:, t, e:e + 1],
                                           in1=x1[:, t, :], op0=ALU.mult, op1=ALU.add).then_inc(v_ME, 1)

            def xq():
                count = [0]

                def link(ins, held=True):
                    count[0] += 1
                    ins.then_inc(v_xq, 1)
                    if held:
                        dve.wait_ge(v_xq, n("XQ", XQ_OPS, count[0]))

                dve.wait_ge(v_ln, n("LN", LN_OPS))
                dve.wait_ge(a_F1, n("F1"))
                dve.wait_ge(pe_XB, n("XB"))
                link(v.tensor_reduce(am[:, 0, :], xn[:], AX.X, ALU.max, apply_absolute_value=True))
                link(v.tensor_scalar(am[:, 0, :], am[:, 0, :], Q_EPS, None, ALU.max))
                link(v.tensor_scalar(am[:, 2, :], am[:, 0, :], dqf[:, 0:1], None, ALU.mult))
                link(v.reciprocal(am[:, 1, :], am[:, 0, :]))
                link(v.tensor_scalar(am[:, 1, :], am[:, 1, :], 127.0, None, ALU.mult))
                for t in range(NT):
                    link(v.tensor_scalar(xn[:, t, :], xn[:, t, :], am[:, 1, t:t + 1], MAGIC, ALU.mult, ALU.add),
                         held=t == NT - 1)
                for k in range(2):
                    link(v.tensor_scalar(xi[:, 2 * k:2 * k + 2, :].rearrange("p a b -> p (a b)"),
                                         xn[:, 2 * k:2 * k + 2, :].rearrange("p a b -> p (a b)"), MAGIC, None,
                                         ALU.subtract), held=False)
                assert count[0] == XQ_OPS

            def hquant(t):
                count = [0]

                def link(ins):
                    count[0] += 1
                    ins.then_inc(v_hq, 1)
                    dve.wait_ge(v_hq, n("HQ", HQ_OPS, count[0]))

                dve.wait_ge(a_F1, n("F1", 1, 2 * t + 2 - 2 * NT))
                dve.wait_ge(pe_HT, n("HQ", 1, -min(t, 1)))
                dve.wait_ge(v_F2, n("F2"))
                big, inv, deq = am[:, 4, t:t + 1], am[:, 5, t:t + 1], am[:, 3, t:t + 1]
                link(v.tensor_reduce(big, hh[:, t, :], AX.X, ALU.max, apply_absolute_value=True))
                link(v.tensor_scalar(big, big, Q_EPS, None, ALU.max))
                link(v.tensor_scalar(deq, big, dqf[:, 1:2], None, ALU.mult))
                link(v.reciprocal(inv, big))
                link(v.tensor_scalar(inv, inv, 127.0, None, ALU.mult))
                v.tensor_scalar(hr[:], hh[:, t, :], inv, MAGIC, ALU.mult, ALU.add).then_inc(v_hr, 1)
                dve.wait_ge(v_hr, n("HQ", 1, 1))
                link(v.tensor_scalar(hq[:, t % 2, :], hr[:], MAGIC, None, ALU.subtract))
                assert count[0] == HQ_OPS

            def f2(t):
                o = bank()
                dve.wait_ge(pe_F2, n("F2", 1, 1))
                dve.wait_ge(v_ln, n("LN", LN_OPS))
                v.scalar_tensor_tensor(out=x1[:, t, :], in0=o[:, 0:D], scalar=am[:, 3, t:t + 1], in1=x1[:, t, :],
                                       op0=ALU.mult, op1=ALU.add).then_inc(v_F2, 1)

            program(dve, {"INIT": init, "LOAD0": reset, "LN": ln, "SPLIT": split, "VV": vv, "XT": skip, "PREP": prep,
                          "LEAD": maxima, "PERIOD": reset, "HEAD": head, "NT": norm, "OT": skip, "OP": op,
                          "RT": router, "ME": experts, "XQ": xq, "XB": skip, "F1": skip, "HQ": hquant, "HT": skip,
                          "F2": f2}, n)


def kernel(**inputs):
    import numpy as np
    import concourse.bacc as bacc
    from concourse.bass_utils import run_bass_kernel_spmd

    nc = bacc.Bacc("TRN2", target_bir_lowering=False, num_devices=1)
    arrays = {}

    def arg(name, a):
        a = np.ascontiguousarray(a)
        arrays["in_" + name] = a
        return nc.dram_tensor("in_" + name, a.shape, mybir.dt.from_np(a.dtype), kind="ExternalInput").ap()

    def both(key, turn):
        out = []
        for l in range(L):
            a = np.asarray(inputs[f"L{l}_xattn_{key}"])
            if key in ("bq", "bk"):
                a = a.reshape(NC, P)
            out.append(arg(f"{key}{l}", a.T if turn else a))
        return out

    x = arg("x", inputs["x"])
    ctxT = arg("ctxT", np.asarray(inputs["ctx_1024"]).transpose(0, 2, 1))
    gx, gf = arg("g_xattn", inputs["g_xattn"]), arg("g_ffn", inputs["g_ffn"])
    wq, bq, wk, bk = both("Wq", True), both("bq", True), both("Wk", True), both("bk", True)
    wv, bv, wo, bo = both("Wv", True), both("bv", False), both("Wo", True), both("bo", False)
    rw = arg("router_w", np.asarray(inputs["L0_ffn_router_w"]).T)
    rb = arg("router_b", inputs["L0_ffn_router_b"])
    ew = arg("experts", np.asarray(inputs["L0_ffn_expert_weights"]).transpose(1, 0, 2).reshape(D, NE * D))
    w1 = arg("w1", np.asarray(inputs["L1_ffn_w1"]).T)
    w2 = arg("w2", np.asarray(inputs["L1_ffn_w2"]).T)
    out = nc.dram_tensor("out", (B, S, D), F32, kind="ExternalOutput").ap()
    build(nc, x, ctxT, gx, gf, wq, bq, wk, bk, wv, bv, wo, bo, rw, rb, ew, w1, w2, out)
    r = run_bass_kernel_spmd(nc, [arrays], core_ids=[0])
    return r.results[0]["out"]
```
